# Optimizing a Trainium2 kernel written in Bass

```python
import numpy as np
import jax
import jax.numpy as jnp

def _softmax(x, axis=-1):
    return jax.nn.softmax(x, axis=axis)

def _gelu(x):
    return jax.nn.gelu(x, approximate=True)

def _silu(x):
    return jax.nn.silu(x)

def _sigmoid(x):
    return jax.nn.sigmoid(x)

def _layernorm(x, axis=-1, eps=1e-05):
    m = jnp.mean(x, axis=axis, keepdims=True)
    v = jnp.var(x, axis=axis, keepdims=True)
    return (x - m) / jnp.sqrt(v + eps)

def _scatter_add(tgt, idx, src, axis=0):
    return tgt.at[idx].add(src)

def _segment_sum(src, seg, n):
    return jax.ops.segment_sum(src, seg, n)
kernel_name = 'mk_adj_resnorm_d1_adj_r2_208f80'

def setup_inputs(seed: int=0):
    np.random.seed(seed)
    _w = jnp.asarray

    def _rec_inputs():
        import jax
        import jax.numpy as jnp
        _gk = jax.random.key(seed)
        x = 0.0001732 + 1 * jax.random.normal(jax.random.fold_in(_gk, 1), (5120, 64), jnp.float32)
        _a = jax.random.bernoulli(jax.random.fold_in(_gk, 2), 0.00078125, (5120, 5120))
        _af = _a.astype(jnp.float32)
        _af = _af * jax.random.uniform(jax.random.fold_in(_gk, 3), (5120, 5120), jnp.float32, 0.05, 0.02)
        adj = _af
        return (x, adj)
    x, adj = _rec_inputs()

    def _L0_gnn_setup():
        import jax, jax.numpy as jnp
        import numpy as np
        N_USERS = 2048
        N_ITEMS = 3072
        EMB = 64
        LN_EPS = 1e-05
        key = jax.random.key(seed)
        ks = jax.random.split(key, 10)
        N = N_USERS + N_ITEMS
        ego = jax.random.normal(ks[0], (N, EMB), jnp.float32)
        adj = (jax.random.uniform(ks[1], (N, N), jnp.float32) < 0.01).astype(jnp.float32) * 0.02
        xav = float(np.sqrt(6.0 / (EMB + EMB)))
        W_u = jax.random.uniform(ks[2], (EMB, EMB), jnp.float32, -xav, xav)
        W_i = jax.random.uniform(ks[3], (EMB, EMB), jnp.float32, -xav, xav)
        diag_u = jax.random.uniform(ks[4], (N_USERS,), jnp.float32, 0.99, 1.01)
        diag_i = jax.random.uniform(ks[5], (N_ITEMS,), jnp.float32, 0.99, 1.01)
        par_u = jax.random.uniform(ks[6], (2,), jnp.float32, 0.0, 0.99)
        par_i = jax.random.uniform(ks[7], (2,), jnp.float32, 0.0, 0.99)
        ln_gamma = jnp.ones((EMB,), jnp.float32)
        ln_beta = jnp.zeros((EMB,), jnp.float32)
        return {'ego_embeddings': ego, 'adj': adj, 'W_u': W_u, 'diag_u': diag_u, 'par_u': par_u, 'W_i': W_i, 'diag_i': diag_i, 'par_i': par_i, 'ln_gamma': ln_gamma, 'ln_beta': ln_beta}
    _L0_gnn_all = _L0_gnn_setup()
    _L0_gnn_in = {k: v for k, v in _L0_gnn_all.items() if k in ('W_u', 'diag_u', 'par_u', 'W_i', 'diag_i', 'par_i', 'ln_gamma', 'ln_beta')}
    del _L0_gnn_all
    return {'x': x, 'adj': adj, 'L0_gnn_W_u': _L0_gnn_in['W_u'], 'L0_gnn_diag_u': _L0_gnn_in['diag_u'], 'L0_gnn_par_u': _L0_gnn_in['par_u'], 'L0_gnn_W_i': _L0_gnn_in['W_i'], 'L0_gnn_diag_i': _L0_gnn_in['diag_i'], 'L0_gnn_par_i': _L0_gnn_in['par_i'], 'L0_gnn_ln_gamma': _L0_gnn_in['ln_gamma'], 'L0_gnn_ln_beta': _L0_gnn_in['ln_beta']}

def reference(x, adj, L0_gnn_W_u, L0_gnn_diag_u, L0_gnn_par_u, L0_gnn_W_i, L0_gnn_diag_i, L0_gnn_par_i, L0_gnn_ln_gamma, L0_gnn_ln_beta):
    import jax
    import jax.numpy as jnp

    def _L0_gnn_ref(ego_embeddings, adj, W_u, diag_u, par_u, W_i, diag_i, par_i, ln_gamma, ln_beta):
        import jax, jax.numpy as jnp
        import numpy as np
        N_USERS = 2048
        N_ITEMS = 3072
        EMB = 64
        LN_EPS = 1e-05
        nu = diag_u.shape[0]
        res = ego_embeddings
        ego_u = ego_embeddings[:nu]
        ego_i = ego_embeddings[nu:]
        u = par_u[0] * par_u[1] * (diag_u[:, None] * ego_u @ W_u) + ego_u
        i = par_i[0] * par_i[1] * (diag_i[:, None] * ego_i @ W_i) + ego_i
        e = jnp.concatenate([u, i], axis=0)
        h = adj @ (adj.T @ e)
        mu = jnp.mean(h, axis=-1, keepdims=True)
        var = jnp.var(h, axis=-1, keepdims=True)
        out = (h - mu) * jax.lax.rsqrt(var + LN_EPS) * ln_gamma + ln_beta + res
        return out
    x = _layernorm(x + _L0_gnn_ref(x, adj, L0_gnn_W_u, L0_gnn_diag_u, L0_gnn_par_u, L0_gnn_W_i, L0_gnn_diag_i, L0_gnn_par_i, L0_gnn_ln_gamma, L0_gnn_ln_beta), axis=-1)
    return x

_drawn_inputs = setup_inputs


def setup_inputs(seed=0):
    import zlib

    import numpy as np

    out = dict(_drawn_inputs(seed))
    spreads = {'L0_gnn_ln_gamma': (1.0, 0.2), 'L0_gnn_ln_beta': (0.0, 0.1)}
    factors = {'L0_gnn_diag_u': 8.0, 'L0_gnn_W_i': 6.328, 'L0_gnn_diag_i': 8.0}
    for name, (base, spread) in spreads.items():
        noise = np.random.default_rng([zlib.crc32(name.encode()), seed]).standard_normal(out[name].shape)
        drawn = base * np.exp(spread * noise) if base else spread * noise
        out[name] = jnp.asarray(drawn.astype(out[name].dtype))
    for name, factor in factors.items():
        out[name] = (out[name] * factor).astype(out[name].dtype)
    return out
```

```python
from contextlib import ExitStack

import concourse.bass as bass
from concourse import mybir

F32 = mybir.dt.float32
BF16 = mybir.dt.bfloat16
ALU = mybir.AluOpType
ACT = mybir.ActivationFunctionType
AX_X = mybir.AxisListType.X

P = 128
V = 4
QUAD = P * V
BLOCK = 512
M = BLOCK // P
EPS = 1e-5


def build(nc, x, adj, W_u, diag_u, par_u, W_i, diag_i, par_i, gamma, beta, out):
    N, D = x.shape
    NU = diag_u.shape[0]
    QUADS = N // QUAD
    PAIRS = QUADS // 2
    BLOCKS = N // BLOCK
    UQ = NU // QUAD
    UP = UQ // 2
    TILES = QUADS * V
    G = 2 * V
    LN_STEPS = 10
    assert N % (2 * QUAD) == 0 and N % BLOCK == 0 and NU % (2 * QUAD) == 0 and 2 * D == P

    x_rows = x.rearrange("(q p v) f -> p q v f", p=P, v=V)
    out_rows = out.rearrange("(q p v) f -> p q v f", p=P, v=V)
    adj_rows = adj.rearrange("(q p v) c -> q p v c", p=P, v=V)

    with ExitStack() as ctx:
        def sb(name, shape, dt=F32):
            return ctx.enter_context(nc.sbuf_tensor(name, shape, dt))

        def sem(name):
            return ctx.enter_context(nc.semaphore(name))

        raw = sb("raw", [P, QUADS, V, BLOCK])
        adjT = sb("adjT", [P, QUADS, M, QUAD])
        x_sb = sb("x_sb", [P, QUADS, V, D])
        e_sb = sb("e_sb", [P, QUADS, V, D])
        xT = sb("xT", [P, PAIRS, 512])
        yT = sb("yT", [P, PAIRS, 512])
        hT = xT
        x2 = yT[:, :, :].rearrange("p b (g f) -> p (b g) f", f=D)
        tT_sb = sb("tT_sb", [P, BLOCK])
        t_sb = sb("t_sb", [P, M, D])
        ident = sb("ident", [P, P])
        w2 = sb("w2", [P, 2, P])
        zeros = sb("zeros", [P, 512], BF16)
        scale = sb("scale", [P, QUADS, V])
        par = sb("par", [P, 2, 2])
        par01 = sb("par01", [P, 2])
        gb = sb("gb", [P, 2, D])
        eps = sb("eps", [P, 1])
        stat = sb("stat", [P, PAIRS, 8, G])

        h_ps = ctx.enter_context(nc.psum_tensor("h_ps", [P, PAIRS, 512], F32))
        t_ps = ctx.enter_context(nc.psum_tensor("t_ps", [P, BLOCK], F32))
        tr_ps = ctx.enter_context(nc.psum_tensor("tr_ps", [P, 2, 512], F32))

        raw_loaded = [sem(f"raw_loaded{q}") for q in range(QUADS)]
        x_loaded = sem("x_loaded")
        small_loaded = sem("small_loaded")
        w_loaded = sem("w_loaded")
        w2_zeroed = sem("w2_zeroed")
        constants_ready = sem("constants_ready")
        ident_zero = sem("ident_zero")
        ident_ready = sem("ident_ready")
        xT_done = sem("xT_done")
        xT_copied = sem("xT_copied")
        yT_done = sem("yT_done")
        yT_copied = sem("yT_copied")
        y_done = sem("y_done")
        y_scaled = sem("y_scaled")
        par_ready = sem("par_ready")
        scale_ready = sem("scale_ready")
        e_ready = sem("e_ready")
        tile_transposed = sem("tile_transposed")
        tile_stored = sem("tile_stored")
        gather_done = sem("gather_done")
        gather_copied = sem("gather_copied")
        t_turned = sem("t_turned")
        t_ready = sem("t_ready")
        spread_done = sem("spread_done")
        hT_copied = sem("hT_copied")
        h_turned = sem("h_turned")
        x2_ready = sem("x2_ready")
        ln_step = sem("ln_step")
        ln_squared = sem("ln_squared")
        ln_rooted = sem("ln_rooted")
        ln_affine = sem("ln_affine")
        out_stored = sem("out_stored")

        block = ctx.enter_context(nc.Block())

        def wait(eng, s, n):
            if not isinstance(n, int) or n > 0:
                eng.wait_ge(s, n)

        def bank_tiles(b, c):
            return 2 * b + c // 2, 2 * (c % 2)

        @block.sync
        def _(sp):
            def load(j, q):
                wait(sp, tile_transposed, (j - 1) * TILES + V * (q + 1))
                sp.dma_start(raw[:, q, :, :], adj_rows[q, :, :, bass.ds(j * BLOCK, BLOCK)])\
                    .then_inc(raw_loaded[q], 16)

            sp.dma_start(x_sb[:, :, :, :], x_rows).then_inc(x_loaded, 16)
            for q in range(QUADS):
                load(0, q)
            with sp.Fori(1, BLOCKS) as j:
                for q in range(QUADS):
                    load(j, q)
            for b in range(PAIRS):
                sp.wait_ge(ln_step, LN_STEPS * (b + 1))
                sp.dma_start(out_rows[:, 2 * b:2 * b + 2, :, :], e_sb[:, 2 * b:2 * b + 2, :, :])\
                    .then_inc(out_stored, 16)
            sp.wait_ge(out_stored, 16 * PAIRS)

        @block.gpsimd
        def _(pool):
            nc.gpsimd.memset(ident[:, :], 0.0).then_inc(ident_zero, 1)
            nc.gpsimd.memset(w2[:, :, :], 0.0).then_inc(w2_zeroed, 1)
            pool.wait_ge(ident_zero, 1)
            nc.gpsimd.affine_select(out=ident[:, :], in_=ident[:, :], compare_op=ALU.not_equal, fill=1.0,
                                    base=0, pattern=[[-1, P]], channel_multiplier=1).then_inc(ident_ready, 1)
            for b in range(PAIRS):
                pool.wait_ge(y_scaled, b + 1)
                s = e_sb[:, 2 * b:2 * b + 2, :, :]
                nc.gpsimd.tensor_tensor(s, s, x_sb[:, 2 * b:2 * b + 2, :, :], ALU.add).then_inc(e_ready, 1)
            pool.wait_ge(y_done, PAIRS)
            pool.wait_ge(small_loaded, 16 * 6)
            xg = x_sb[:, :, :, :].rearrange("p q v f -> p (q v) f")
            nc.gpsimd.tensor_tensor(x2, xg, xg, ALU.add).then_inc(x2_ready, 1)
            pool.wait_ge(x2_ready, 1)
            nc.gpsimd.tensor_tensor(x2, x2, gb[:, 1:2, :].to_broadcast([P, TILES, D]), ALU.add).then_inc(x2_ready, 1)
            for b in range(PAIRS):
                pool.wait_ge(ln_step, LN_STEPS * b + 5)
                hb = e_sb[:, 2 * b:2 * b + 2, :, :].rearrange("p q v f -> p (q v) f")
                nc.gpsimd.tensor_tensor(hb, hb, gb[:, 0:1, :].to_broadcast([P, G, D]), ALU.mult).then_inc(ln_affine, 1)
                pool.wait_ge(ln_affine, 2 * b + 1)
                if b == 0:
                    pool.wait_ge(x2_ready, 2)
                nc.gpsimd.tensor_tensor(hb, hb, x2[:, G * b:G * b + G, :], ALU.add).then_inc(ln_affine, 1)

        @block.scalar
        def _(act):
            act.wait_ge(w2_zeroed, 1)
            for k, w in enumerate((W_u, W_i)):
                for a in range(2):
                    act.dma_start(w2[D * a:D * a + D, k, D * a:D * a + D], w).then_inc(w_loaded, 16)
            for k, p in enumerate((par_u, par_i)):
                act.dma_start(par[:, k, :], p.partition_broadcast(P)).then_inc(small_loaded, 16)
            for a, b, d in ((0, UQ, diag_u), (UQ, QUADS, diag_i)):
                act.dma_start(scale[:, a:b, :], d.rearrange("(q p v) -> p q v", p=P, v=V)).then_inc(small_loaded, 16)
            for k, g in enumerate((gamma, beta)):
                act.dma_start(gb[:, k, :], g.partition_broadcast(P)).then_inc(small_loaded, 16)
            for b in range(PAIRS):
                act.wait_ge(xT_done, b + 1)
                nc.scalar.copy(xT[:, b, :], h_ps[:, b, :]).then_inc(xT_copied, 1)
            for b in range(PAIRS):
                act.wait_ge(yT_done, b + 1)
                nc.scalar.copy(yT[:, b, :], h_ps[:, b, :]).then_inc(yT_copied, 1)

            def store(j, b):
                for u in range(G):
                    act.wait_ge(tile_transposed, j * TILES + G * b + u + 1)
                    nc.scalar.copy(adjT[:, 2 * b + u // V, :, P * (u % V):P * (u % V) + P],
                                   tr_ps[:, u % 2, :].rearrange("p (m r) -> p m r", r=P)).then_inc(tile_stored, 1)

            for b in range(PAIRS - 1):
                store(0, b)
            with act.Fori(1, BLOCKS) as j:
                store(j - 1, PAIRS - 1)
                for b in range(PAIRS - 1):
                    store(j, b)
            store(BLOCKS - 1, PAIRS - 1)
            act.wait_ge(constants_ready, 2)

            def copy_hT(b):
                act.wait_ge(spread_done, b + 1)
                nc.scalar.copy(hT[:, b, :], h_ps[:, b, :]).then_inc(hT_copied, 1)

            def square_and_root(b, k):
                z = e_sb[:, 2 * b:2 * b + 2, :, :].rearrange("p q v f -> p (q v f)")
                act.wait_ge(ln_step, LN_STEPS * b + (2, 7)[k])
                nc.scalar.activation(h_ps[:, b, :], z, ACT.Square).then_inc(ln_squared, 1)
                act.wait_ge(ln_step, LN_STEPS * b + (3, 8)[k])
                nc.scalar.activation(stat[:, b, 4 * k + 2, :], stat[:, b, (1, 5)[k], :], ACT.Sqrt,
                                     bias=eps[:, :], scale=1.0 / D).then_inc(ln_rooted, 1)

            for b in range(PAIRS):
                copy_hT(b)
                square_and_root(b, 0)
                square_and_root(b, 1)

        @block.vector
        def _(dve):
            nc.vector.memset(zeros[:, :], 0.0).then_inc(constants_ready, 1)
            nc.vector.memset(eps[:, :], EPS).then_inc(constants_ready, 1)
            dve.wait_ge(small_loaded, 16 * 6)
            nc.vector.tensor_tensor(par01[:, :], par[:, :, 0], par[:, :, 1], ALU.mult).then_inc(par_ready, 1)
            dve.wait_ge(par_ready, 1)
            for k, (a, b) in enumerate(((0, UQ), (UQ, QUADS))):
                nc.vector.tensor_scalar(scale[:, a:b, :], scale[:, a:b, :], par01[:, k:k + 1], None,
                                        ALU.mult).then_inc(scale_ready, 1)
            dve.wait_ge(scale_ready, 2)
            for b in range(PAIRS):
                dve.wait_ge(y_done, b + 1)
                s = scale[:, 2 * b:2 * b + 2, :].rearrange("p q v -> p (q v)").unsqueeze(2).to_broadcast([P, G, D])
                nc.vector.tensor_tensor(e_sb[:, 2 * b:2 * b + 2, :, :].rearrange("p q v f -> p (q v) f"),
                                        h_ps[:, b, :].rearrange("p (g f) -> p g f", f=D), s,
                                        ALU.mult).then_inc(y_scaled, 1)

            def finish_t(j):
                dve.wait_ge(gather_done, j + 1)
                nc.vector.tensor_copy(tT_sb[:, :], t_ps[:, :]).then_inc(gather_copied, 1)
                for half in range(2):
                    dve.wait_ge(t_turned, 2 * j + half + 1)
                    nc.vector.tensor_reduce(
                        t_sb[:, 2 * half:2 * half + 2, :],
                        tr_ps[:, half, 0:2 * P].rearrange("p (m s f) -> p m f s", m=2, s=2),
                        AX_X, ALU.add).then_inc(t_ready, 1)

            with dve.Fori(0, BLOCKS) as j:
                finish_t(j)

            for b in range(PAIRS):
                at = LN_STEPS * b
                zg = e_sb[:, 2 * b:2 * b + 2, :, :].rearrange("p q v f -> p (q v) f")
                h = h_ps[:, b, :].rearrange("p (g f) -> p g f", f=D)
                squares = h_ps[:, b, :].rearrange("p (g f) -> p g f", f=D)

                def row_stat(k):
                    return stat[:, b, k, :]

                def over_row(k):
                    return row_stat(k).unsqueeze(2).to_broadcast([P, G, D])

                def step(k, ins):
                    ins.then_inc(ln_step, 1)
                    if k in (1, 4, 6, 9):
                        dve.wait_ge(ln_step, at + k)

                dve.wait_ge(h_turned, b + 1)
                step(1, nc.vector.tensor_reduce(row_stat(0), h, AX_X, ALU.add))
                step(2, nc.vector.scalar_tensor_tensor(zg, over_row(0), -1.0 / D, h, ALU.mult, ALU.add))
                dve.wait_ge(ln_squared, 2 * b + 1)
                step(3, nc.vector.tensor_reduce(row_stat(1), squares, AX_X, ALU.add))
                dve.wait_ge(ln_rooted, 2 * b + 1)
                step(4, nc.vector.reciprocal(row_stat(3), row_stat(2)))
                step(5, nc.vector.tensor_tensor(zg, zg, over_row(3), ALU.mult))
                dve.wait_ge(ln_affine, 2 * b + 2)
                step(6, nc.vector.tensor_reduce(row_stat(4), zg, AX_X, ALU.add))
                step(7, nc.vector.scalar_tensor_tensor(zg, over_row(4), -1.0 / D, zg, ALU.mult, ALU.add))
                dve.wait_ge(ln_squared, 2 * b + 2)
                step(8, nc.vector.tensor_reduce(row_stat(5), squares, AX_X, ALU.add))
                dve.wait_ge(ln_rooted, 2 * b + 2)
                step(9, nc.vector.reciprocal(row_stat(7), row_stat(6)))
                step(10, nc.vector.tensor_tensor(zg, zg, over_row(7), ALU.mult))

        @block.tensor
        def _(pe):
            pe.wait_ge(ident_ready, 1)
            pe.wait_ge(x_loaded, 16)
            for b in range(PAIRS):
                for c in range(4):
                    q, v = bank_tiles(b, c)
                    last = nc.tensor.transpose(h_ps[:, b, P * c:P * c + P],
                                               x_sb[:, q, v:v + 2, :].rearrange("p v f -> p (v f)"), ident[:, :])
                last.then_inc(xT_done, 1)
            pe.wait_ge(w_loaded, 16 * 4)
            for b in range(PAIRS):
                pe.wait_ge(xT_copied, b + 1)
                nc.tensor.matmul(h_ps[:, b, :], w2[:, 0 if b < UP else 1, :], xT[:, b, :],
                                 start=True, stop=True).then_inc(yT_done, 1)
            for b in range(PAIRS):
                pe.wait_ge(yT_copied, b + 1)
                for c in range(4):
                    last = nc.tensor.transpose(h_ps[:, b, P * c:P * c + P], yT[:, b, P * c:P * c + P], ident[:, :])
                last.then_inc(y_done, 1)

            def gather(j, b, c):
                q, v = bank_tiles(b, c)
                if c % 2 == 0:
                    pe.wait_ge(raw_loaded[q], 16 * (j + 1))
                for k in range(2):
                    last = nc.tensor.matmul(t_ps[D * k:D * k + D, :], e_sb[:, q, v + k, :], raw[:, q, v + k, :],
                                            start=(b == 0 and c == 0), stop=(b == PAIRS - 1 and c == 3))
                if b == PAIRS - 1 and c == 3:
                    last.then_inc(gather_done, 1)

            def turn_tile(j, b, u):
                wait(pe, tile_stored, j * TILES + G * b + u - 1)
                for m in range(M):
                    last = nc.tensor.transpose(tr_ps[:, u % 2, P * m:P * m + P],
                                               raw[:, 2 * b + u // V, u % V, P * m:P * m + P], ident[:, :])
                last.then_inc(tile_transposed, 1)

            def turn_t(j, half):
                if half == 0:
                    pe.wait_ge(gather_copied, j + 1)
                pe.wait_ge(tile_stored, j * TILES + G * (PAIRS - 1) + half + 1)
                for m in range(2):
                    last = nc.tensor.transpose(tr_ps[:, half, P * m:P * m + P],
                                               tT_sb[:, P * (2 * half + m):P * (2 * half + m + 1)], ident[:, :])
                last.then_inc(t_turned, 1)

            def spread(j, b, m):
                if m == 0:
                    pe.wait_ge(tile_stored, j * TILES + G * (b + 1))
                for k in range(2):
                    last = nc.tensor.matmul(h_ps[D * k:D * k + D, b, :], t_sb[:, m, :], adjT[:, 2 * b + k, m, :],
                                            start=False, stop=(m == M - 1), skip_group_check=True)
                return last

            def turn_over(j, more):
                b = PAIRS - 1

                def gather_more(c):
                    if more:
                        gather(j + 1, 0, c)

                turn_tile(j, b, 0)
                turn_tile(j, b, 1)
                turn_t(j, 0)
                turn_t(j, 1)
                gather_more(0)
                for half in range(2):
                    pe.wait_ge(t_ready, 2 * j + half + 1)
                    turn_tile(j, b, 2 + half)
                gather_more(1)
                turn_tile(j, b, 4)
                spread(j, 0, 0)
                turn_tile(j, b, 5)
                gather_more(2)
                spread(j, 0, 1)
                turn_tile(j, b, 6)
                gather_more(3)
                spread(j, 0, 2)
                turn_tile(j, b, 7)
                return spread(j, 0, 3)

            for b in range(PAIRS):
                pe.wait_ge(e_ready, b + 1)
                for c in range(4):
                    gather(0, b, c)
                    if b > 0:
                        turn_tile(0, b - 1, 2 * c)
                        turn_tile(0, b - 1, 2 * c + 1)
            pe.wait_ge(constants_ready, 2)
            for b in range(PAIRS):
                nc.tensor.matmul(h_ps[:, b, :], zeros[:, 0:P], zeros[:, :], start=True, stop=True)

            with pe.Fori(1, BLOCKS) as j:
                turn_over(j - 1, True)
                for b in range(1, PAIRS):
                    for c in range(4):
                        gather(j, b, c)
                        turn_tile(j, b - 1, 2 * c)
                        spread(j - 1, b, c)
                        turn_tile(j, b - 1, 2 * c + 1)

            def turn_h(b):
                pe.wait_ge(hT_copied, b + 1)
                rows = h_ps[:, b, :].rearrange("p (s v f) -> p v s f", s=2, v=V)
                for v in range(V):
                    last = nc.tensor.transpose(rows[:, v, :, :], hT[:, b, P * v:P * v + P], ident[:, :])
                last.then_inc(h_turned, 1)

            turn_over(BLOCKS - 1, False).then_inc(spread_done, 1)
            for b in range(1, PAIRS):
                for m in range(M):
                    last = spread(BLOCKS - 1, b, m)
                last.then_inc(spread_done, 1)
                turn_h(b - 1)
            turn_h(PAIRS - 1)


_NAMES = ["x", "adj", "L0_gnn_W_u", "L0_gnn_diag_u", "L0_gnn_par_u", "L0_gnn_W_i", "L0_gnn_diag_i",
          "L0_gnn_par_i", "L0_gnn_ln_gamma", "L0_gnn_ln_beta"]


def kernel(**inputs):
    import numpy as np
    import concourse.bacc as bacc
    from concourse.bass_utils import run_bass_kernel_spmd

    nc = bacc.Bacc("TRN2", target_bir_lowering=False, num_devices=1)
    arrays, args = {}, []
    for name in _NAMES:
        a = np.ascontiguousarray(inputs[name])
        arrays[f"in_{name}"] = a
        args.append(nc.dram_tensor(f"in_{name}", a.shape, mybir.dt.from_np(a.dtype), kind="ExternalInput").ap())
    out = nc.dram_tensor("out_0", inputs["x"].shape, F32, kind="ExternalOutput").ap()
    build(nc, *args, out)
    r = run_bass_kernel_spmd(nc, [arrays], core_ids=[0])
    return r.results[0]["out_0"]
```

```python
from contextlib import ExitStack

import concourse.bass as bass
from concourse import mybir

F32 = mybir.dt.float32
BF16 = mybir.dt.bfloat16
ALU = mybir.AluOpType
ACT = mybir.ActivationFunctionType
AX_X = mybir.AxisListType.X

P = 128
S = 32
R = P // S
V = 4
QUAD = P * V
BLOCK = 512
M = BLOCK // P
EPS = 1e-5
PARTS = [(a, (a + d) % R) for d in range(R) for a in range(R)]
SHARES = ((8, 8, 0), (6, 6, 4))
T_AFTER = (4, 5)


def build(nc, x, adj, W_u, diag_u, par_u, W_i, diag_i, par_i, gamma, beta, out):
    N, D = x.shape
    NU = diag_u.shape[0]
    QUADS = N // QUAD
    PAIRS = QUADS // 2
    LAST = PAIRS - 1
    VQ = 2 * LAST
    BLOCKS = N // BLOCK
    UQ = NU // QUAD
    UP = UQ // 2
    G = 2 * V
    assert N % (2 * QUAD) == 0 and N % BLOCK == 0 and NU % (2 * QUAD) == 0 and 2 * D == P

    x_rows = x.rearrange("(q p v) f -> p q v f", p=P, v=V)
    out_rows = out.rearrange("(q p v) f -> p q v f", p=P, v=V)
    adj_rows = adj.rearrange("(q p v) c -> q p v c", p=P, v=V)

    with ExitStack() as ctx:
        def sb(name, shape, dt=F32):
            return ctx.enter_context(nc.sbuf_tensor(name, shape, dt))

        def sem(name):
            return ctx.enter_context(nc.semaphore(name))

        raw = sb("raw", [P, QUADS, V, BLOCK])
        adjT = sb("adjT", [P, QUADS, R, QUAD])
        squares = sb("squares", [P, 2, R, QUAD])
        x_sb = sb("x_sb", [P, QUADS, V, D])
        e_sb = sb("e_sb", [P, QUADS, V, D])
        tT_sb = sb("tT_sb", [P, BLOCK])
        t_sb = sb("t_sb", [P, M, D])
        ident = sb("ident", [P, P])
        centre = sb("centre", [P, 2, D])
        w2 = sb("w2", [P, 2, P])
        zeros = sb("zeros", [P, 512], BF16)
        scale = sb("scale", [P, QUADS, V])
        par = sb("par", [P, 2, 2])
        par01 = sb("par01", [P, 2])
        gb = sb("gb", [P, 2, D])
        eps = sb("eps", [P, 1])
        stat = sb("stat", [P, PAIRS, 7, G])
        xT = adjT[:, 2 * LAST:QUADS, :, :].rearrange("p q i n -> p (q i) n")[:, 0:PAIRS, :]
        yT = e_sb[:, :, :, :].rearrange("p (b q) v f -> p b (q v f)", q=2)
        hT = raw[:, 0:2, :, :].rearrange("p q v c -> p (q v) c")[:, 0:PAIRS, :]

        h_ps = ctx.enter_context(nc.psum_tensor("h_ps", [P, PAIRS, 512], F32))
        t_ps = ctx.enter_context(nc.psum_tensor("t_ps", [P, BLOCK], F32))
        tr_ps = ctx.enter_context(nc.psum_tensor("tr_ps", [P, 2, 512], F32))

        raw_loaded = [sem(f"raw_loaded{q}") for q in range(QUADS)]
        x_loaded = sem("x_loaded")
        w_loaded = sem("w_loaded")
        scale_loaded = sem("scale_loaded")
        gb_loaded = sem("gb_loaded")
        w2_zeroed = sem("w2_zeroed")
        ident_zeroed = sem("ident_zeroed")
        ident_ready = sem("ident_ready")
        centre_set = sem("centre_set")
        centre_ready = sem("centre_ready")
        constants_ready = sem("constants_ready")
        xT_done = sem("xT_done")
        xT_copied = sem("xT_copied")
        yT_done = sem("yT_done")
        yT_copied = sem("yT_copied")
        y_done = sem("y_done")
        y_scaled = sem("y_scaled")
        par_ready = sem("par_ready")
        scale_ready = sem("scale_ready")
        e_ready = sem("e_ready")
        x2_ready = sem("x2_ready")
        quad_gathered = sem("quad_gathered")
        pair_spread = sem("pair_spread")
        quad_squared = sem("quad_squared")
        vector_moved = sem("vector_moved")
        scalar_moved = sem("scalar_moved")
        rest_moved = [sem(f"rest_moved{k}") for k in range(2)]
        REST = 16 * SHARES[1][2]
        tile_turned = sem("tile_turned")
        tile_stored = sem("tile_stored")
        gather_done = sem("gather_done")
        gather_copied = sem("gather_copied")
        t_turned = sem("t_turned")
        t_ready = sem("t_ready")
        hT_copied = sem("hT_copied")
        h_centred = sem("h_centred")
        squared1 = sem("squared1")
        summed1 = sem("summed1")
        rooted1 = sem("rooted1")
        inverted1 = sem("inverted1")
        scaled1 = sem("scaled1")
        times_gamma = sem("times_gamma")
        affine_done = sem("affine_done")
        summed2 = sem("summed2")
        centred2 = sem("centred2")
        squared2 = sem("squared2")
        varied2 = sem("varied2")
        rooted2 = sem("rooted2")
        inverted2 = sem("inverted2")
        out_ready = sem("out_ready")
        out_stored = sem("out_stored")

        block = ctx.enter_context(nc.Block())

        def wait(eng, s, n):
            if not isinstance(n, int) or n > 0:
                eng.wait_ge(s, n)

        def couple(b, c):
            return 2 * b + c // 2, 2 * (c % 2)

        def first(j):
            return isinstance(j, int) and j == 0

        def later_quads(j):
            return range(T_AFTER[0 if first(j) else 1] + 1, VQ)

        def shares(j):
            v, a, d = SHARES[0 if first(j) else 1]
            return PARTS[:v], PARTS[v:v + a], PARTS[v + a:]

        def part(q, k, i, to):
            return squares[S * i:S * i + S, k, to, :], adjT[S * to:S * to + S, q, i, :]

        @block.sync
        def _(sp):
            def load(j, q):
                if q < VQ:
                    if isinstance(j, int) and j == 1:
                        sp.wait_ge(quad_gathered, q + 1)
                    wait(sp, quad_squared, (j - 1) * VQ + q + 1)
                else:
                    wait(sp, tile_turned, (j - 1) * G + V * (q - VQ + 1))
                sp.dma_start(raw[:, q, :, :], adj_rows[q, :, :, bass.ds(j * BLOCK, BLOCK)])\
                    .then_inc(raw_loaded[q], 16)

            def move(j, q):
                for i, to in shares(j)[2]:
                    src, dst = part(q, q % 2, i, to)
                    sp.dma_start(dst, src).then_inc(rest_moved[q % 2], 16)

            sp.dma_start(x_sb[:, :, :, :], x_rows).then_inc(x_loaded, 16)
            sp.wait_ge(w2_zeroed, 1)
            for k, w in enumerate((W_u, W_i)):
                for a in range(2):
                    sp.dma_start(w2[D * a:D * a + D, k, D * a:D * a + D], w).then_inc(w_loaded, 16)
            for q in range(QUADS):
                load(0, q)
            def whole_block(j):
                for q in range(QUADS):
                    load(j + 1, q)
                    if q < VQ and not first(j):
                        move(j, q)

            whole_block(0)
            with sp.Fori(1, BLOCKS - 1) as j:
                whole_block(j)
            for q in range(VQ):
                sp.wait_ge(quad_squared, (BLOCKS - 1) * VQ + q + 1)
                move(BLOCKS - 1, q)
            for b in range(PAIRS):
                sp.wait_ge(out_ready, b + 1)
                sp.dma_start(out_rows[:, 2 * b:2 * b + 2, :, :], e_sb[:, 2 * b:2 * b + 2, :, :])\
                    .then_inc(out_stored, 16)
            sp.wait_ge(out_stored, 16 * PAIRS)

        @block.gpsimd
        def _(pool):
            nc.gpsimd.memset(ident[:, :], 0.0).then_inc(ident_zeroed, 1)
            nc.gpsimd.memset(w2[:, :, :], 0.0).then_inc(w2_zeroed, 1)
            pool.wait_ge(ident_zeroed, 1)
            nc.gpsimd.affine_select(out=ident[:, :], in_=ident[:, :], compare_op=ALU.not_equal, fill=1.0,
                                    base=0, pattern=[[-1, P]], channel_multiplier=1).then_inc(ident_ready, 1)
            for b in range(PAIRS):
                pool.wait_ge(y_scaled, b + 1)
                s = e_sb[:, 2 * b:2 * b + 2, :, :]
                nc.gpsimd.tensor_tensor(s, s, x_sb[:, 2 * b:2 * b + 2, :, :], ALU.add).then_inc(e_ready, 1)
            for k, g in enumerate((gamma, beta)):
                pool.dma_start(gb[:, k, :], g.partition_broadcast(P)).then_inc(gb_loaded, 16)
            pool.wait_ge(e_ready, PAIRS)
            x2 = x_sb[:, :, :, :].rearrange("p q v f -> p (q v) f")
            nc.gpsimd.tensor_tensor(x2, x2, x2, ALU.add).then_inc(x2_ready, 1)
            pool.wait_ge(gb_loaded, 16 * 2)
            pool.wait_ge(x2_ready, 1)
            nc.gpsimd.tensor_tensor(x2, x2, gb[:, 1:2, :].to_broadcast([P, QUADS * V, D]), ALU.add)\
                .then_inc(x2_ready, 1)
            nc.gpsimd.memset(centre[:, :, :], 0.0).then_inc(centre_set, 1)
            pool.wait_ge(centre_set, 1)
            for a in range(2):
                nc.gpsimd.memset(centre[D * a:D * a + D, a, :], -1.0 / D).then_inc(centre_set, 1)
            pool.wait_ge(centre_set, 3)
            cc = centre[:, :, :].rearrange("p a f -> p (a f)")
            nc.gpsimd.tensor_tensor(cc, cc, ident[:, :], ALU.add).then_inc(centre_ready, 1)
            for b in range(PAIRS):
                pool.wait_ge(scaled1, b + 1)
                if b == 0:
                    pool.wait_ge(x2_ready, 2)
                z = e_sb[:, 2 * b:2 * b + 2, :, :].rearrange("p q v f -> p (q v) f")
                nc.gpsimd.tensor_tensor(z, z, gb[:, 0:1, :].to_broadcast([P, G, D]), ALU.mult).then_inc(times_gamma, 1)
                pool.wait_ge(times_gamma, b + 1)
                nc.gpsimd.tensor_tensor(z, z, x2[:, G * b:G * b + G, :], ALU.add).then_inc(affine_done, 1)

        @block.scalar
        def _(act):
            for k, p in enumerate((par_u, par_i)):
                act.dma_start(par[:, k, :], p.partition_broadcast(P)).then_inc(scale_loaded, 16)
            for a, b, d in ((0, UQ, diag_u), (UQ, QUADS, diag_i)):
                act.dma_start(scale[:, a:b, :], d.rearrange("(q p v) -> p q v", p=P, v=V)).then_inc(scale_loaded, 16)
            for b in range(PAIRS):
                act.wait_ge(xT_done, b + 1)
                nc.scalar.copy(xT[:, b, :], h_ps[:, b, :]).then_inc(xT_copied, 1)
            for b in range(PAIRS):
                act.wait_ge(yT_done, b + 1)
                nc.scalar.copy(yT[:, b, :], h_ps[:, b, :]).then_inc(yT_copied, 1)

            def move(j, q):
                act.wait_ge(quad_squared, j * VQ + q + 1)
                last = None
                for i, to in shares(j)[1]:
                    src, dst = part(q, q % 2, i, to)
                    before, last = last, nc.scalar.copy(dst, src)
                last.then_inc(scalar_moved, 1)
                if first(j):
                    before.then_inc(rest_moved[q % 2], REST)

            def store(j, u):
                act.wait_ge(tile_turned, j * G + u + 1)
                nc.scalar.copy(adjT[:, VQ + u // V, :, P * (u % V):P * (u % V) + P],
                               tr_ps[:, u % 2, :].rearrange("p (m r) -> p m r", r=P)).then_inc(tile_stored, 1)

            for q in range(VQ):
                if q not in later_quads(0):
                    move(0, q)
            for u in range(G):
                store(0, u)
            for q in later_quads(0):
                move(0, q)
            for q in range(VQ):
                if q not in later_quads(1):
                    move(1, q)
            with act.Fori(2, BLOCKS) as j:
                for u in range(G):
                    store(j - 1, u)
                for q in later_quads(1):
                    move(j - 1, q)
                for q in range(VQ):
                    if q not in later_quads(1):
                        move(j, q)
            for u in range(G):
                store(BLOCKS - 1, u)
            for q in later_quads(BLOCKS - 1):
                move(BLOCKS - 1, q)

            act.wait_ge(constants_ready, 2)

            def rows(b):
                return e_sb[:, 2 * b:2 * b + 2, :, :].rearrange("p q v f -> p (q v f)")

            def root(b, of, to):
                return nc.scalar.activation(stat[:, b, to, :], stat[:, b, of, :], ACT.Sqrt,
                                            bias=eps[:, :], scale=1.0 / D)

            for n in range(PAIRS + 2):
                if n < PAIRS:
                    act.wait_ge(pair_spread, PAIRS * (BLOCKS - 1) + n + 1)
                    nc.scalar.copy(hT[:, n, :], h_ps[:, n, :]).then_inc(hT_copied, 1)
                    act.wait_ge(h_centred, n + 1)
                    nc.scalar.activation(rows(n), h_ps[:, n, :], ACT.Square).then_inc(squared1, 1)
                    act.wait_ge(summed1, n + 1)
                    root(n, 0, 1).then_inc(rooted1, 1)
                if 0 <= n - 1 < PAIRS:
                    act.wait_ge(centred2, n)
                    nc.scalar.activation(h_ps[:, n - 1, :], rows(n - 1), ACT.Square).then_inc(squared2, 1)
                if 0 <= n - 2:
                    act.wait_ge(varied2, n - 1)
                    root(n - 2, 4, 5).then_inc(rooted2, 1)

        @block.vector
        def _(dve):
            nc.vector.memset(zeros[:, :], 0.0).then_inc(constants_ready, 1)
            nc.vector.memset(eps[:, :], EPS).then_inc(constants_ready, 1)
            def square(j, q):
                k = q % 2
                dve.wait_ge(raw_loaded[q], 16 * (j + 1))
                if k == 0 and not first(j):
                    dve.wait_ge(pair_spread, (j - 1) * PAIRS + q // 2 + 1)
                n = j * VQ + q - 1
                wait(dve, vector_moved, n)
                wait(dve, scalar_moved, n)
                wait(dve, rest_moved[k], REST * (j * (VQ // 2) + q // 2))
                nc.vector.transpose(squares[:, k, :, :].rearrange("p t (a r) -> p a t r", r=S),
                                    raw[:, q, :, :].rearrange("p v (m t c) -> p (v m) t c", t=R, c=S))\
                    .then_inc(quad_squared, 1)

            def move(j, q):
                dve.wait_ge(quad_squared, j * VQ + q + 1)
                for i, to in shares(j)[0]:
                    src, dst = part(q, q % 2, i, to)
                    last = nc.vector.tensor_copy(dst, src)
                last.then_inc(vector_moved, 1)

            def finish_t(j):
                dve.wait_ge(gather_done, j + 1)
                nc.vector.tensor_copy(tT_sb[:, :], t_ps[:, :]).then_inc(gather_copied, 1)
                for half in range(2):
                    dve.wait_ge(t_turned, 2 * j + half + 1)
                    nc.vector.tensor_reduce(
                        t_sb[:, 2 * half:2 * half + 2, :],
                        tr_ps[:, half, 0:2 * P].rearrange("p (m s f) -> p m f s", m=2, s=2),
                        AX_X, ALU.add).then_inc(t_ready, 1)

            EARLY = range(1)
            for q in EARLY:
                square(0, q)
                move(0, q)
            dve.wait_ge(scale_loaded, 16 * 4)
            nc.vector.tensor_tensor(par01[:, :], par[:, :, 0], par[:, :, 1], ALU.mult).then_inc(par_ready, 1)
            dve.wait_ge(par_ready, 1)
            for k, (a, b) in enumerate(((0, UQ), (UQ, QUADS))):
                nc.vector.tensor_scalar(scale[:, a:b, :], scale[:, a:b, :], par01[:, k:k + 1], None,
                                        ALU.mult).then_inc(scale_ready, 1)
            dve.wait_ge(scale_ready, 2)
            for b in range(PAIRS):
                dve.wait_ge(y_done, b + 1)
                s = scale[:, 2 * b:2 * b + 2, :].rearrange("p q v -> p (q v)").unsqueeze(2).to_broadcast([P, G, D])
                nc.vector.tensor_tensor(e_sb[:, 2 * b:2 * b + 2, :, :].rearrange("p q v f -> p (q v) f"),
                                        h_ps[:, b, :].rearrange("p (g f) -> p g f", f=D), s,
                                        ALU.mult).then_inc(y_scaled, 1)

            def whole_block(j):
                for q in range(VQ):
                    if not (first(j) and q in EARLY):
                        square(j, q)
                        move(j, q)
                    if q + 1 == later_quads(j)[0]:
                        finish_t(j)

            whole_block(0)
            with dve.Fori(1, BLOCKS) as j:
                whole_block(j)

            def over_row(b, k):
                return stat[:, b, k, :].unsqueeze(2).to_broadcast([P, G, D])

            def bank(b):
                return h_ps[:, b, :].rearrange("p (g f) -> p g f", f=D)

            def rows(b):
                return e_sb[:, 2 * b:2 * b + 2, :, :].rearrange("p q v f -> p (q v) f")

            def first_norm(b):
                dve.wait_ge(squared1, b + 1)
                nc.vector.tensor_reduce(stat[:, b, 0, :], rows(b), AX_X, ALU.add).then_inc(summed1, 1)
                dve.wait_ge(rooted1, b + 1)
                nc.vector.reciprocal(stat[:, b, 2, :], stat[:, b, 1, :]).then_inc(inverted1, 1)
                dve.wait_ge(inverted1, b + 1)
                nc.vector.tensor_tensor(rows(b), bank(b), over_row(b, 2), ALU.mult).then_inc(scaled1, 1)

            def second_mean(b):
                dve.wait_ge(affine_done, b + 1)
                nc.vector.tensor_reduce(stat[:, b, 3, :], rows(b), AX_X, ALU.add).then_inc(summed2, 1)
                dve.wait_ge(summed2, b + 1)
                nc.vector.scalar_tensor_tensor(rows(b), over_row(b, 3), -1.0 / D, rows(b), ALU.mult, ALU.add)\
                    .then_inc(centred2, 1)

            def second_norm(b):
                dve.wait_ge(squared2, b + 1)
                nc.vector.tensor_reduce(stat[:, b, 4, :], bank(b), AX_X, ALU.add).then_inc(varied2, 1)
                dve.wait_ge(rooted2, b + 1)
                nc.vector.reciprocal(stat[:, b, 6, :], stat[:, b, 5, :]).then_inc(inverted2, 1)
                dve.wait_ge(inverted2, b + 1)
                nc.vector.tensor_tensor(rows(b), rows(b), over_row(b, 6), ALU.mult).then_inc(out_ready, 1)

            for n in range(PAIRS + 2):
                if n < PAIRS:
                    first_norm(n)
                if 0 <= n - 1 < PAIRS:
                    second_mean(n - 1)
                if 0 <= n - 2:
                    second_norm(n - 2)

        @block.tensor
        def _(pe):
            pe.wait_ge(ident_ready, 1)
            pe.wait_ge(x_loaded, 16)
            for b in range(PAIRS):
                for c in range(4):
                    q, v = couple(b, c)
                    last = nc.tensor.transpose(h_ps[:, b, P * c:P * c + P],
                                               x_sb[:, q, v:v + 2, :].rearrange("p v f -> p (v f)"), ident[:, :])
                last.then_inc(xT_done, 1)
            pe.wait_ge(w_loaded, 16 * 4)
            for b in range(PAIRS):
                pe.wait_ge(xT_copied, b + 1)
                nc.tensor.matmul(h_ps[:, b, :], w2[:, 0 if b < UP else 1, :], xT[:, b, :],
                                 start=True, stop=True).then_inc(yT_done, 1)
            for b in range(PAIRS):
                pe.wait_ge(yT_copied, b + 1)
                for c in range(4):
                    last = nc.tensor.transpose(h_ps[:, b, P * c:P * c + P], yT[:, b, P * c:P * c + P], ident[:, :])
                last.then_inc(y_done, 1)

            def gather(j, b, c):
                q, v = couple(b, c)
                if c % 2 == 0:
                    pe.wait_ge(raw_loaded[q], 16 * (j + 1))
                for k in range(2):
                    last = nc.tensor.matmul(t_ps[D * k:D * k + D, :], e_sb[:, q, v + k, :], raw[:, q, v + k, :],
                                            start=(b == 0 and c == 0), stop=(b == LAST and c == 3))
                if b == LAST and c == 3:
                    last.then_inc(gather_done, 1)
                elif c % 2 == 1 and b < LAST and isinstance(j, int):
                    last.then_inc(quad_gathered, 1)

            def turn_tile(j, u):
                if u >= 2:
                    pe.wait_ge(tile_stored, j * G + u - 1)
                for m in range(M):
                    last = nc.tensor.transpose(tr_ps[:, u % 2, P * m:P * m + P],
                                               raw[:, VQ + u // V, u % V, P * m:P * m + P], ident[:, :])
                last.then_inc(tile_turned, 1)

            def turn_t(j, half):
                if half == 0:
                    pe.wait_ge(gather_copied, j + 1)
                pe.wait_ge(tile_stored, j * G + half + 1)
                for m in range(2):
                    last = nc.tensor.transpose(tr_ps[:, half, P * m:P * m + P],
                                               tT_sb[:, P * (2 * half + m):P * (2 * half + m + 1)], ident[:, :])
                last.then_inc(t_turned, 1)

            def spread(j, b, m):
                if m == 0 and b < LAST:
                    pe.wait_ge(vector_moved, j * VQ + 2 * b + 2)
                    pe.wait_ge(scalar_moved, j * VQ + 2 * b + 2)
                    for k in range(2):
                        pe.wait_ge(rest_moved[k], REST * (j * (VQ // 2) + b + 1))
                if m == 0 and b == LAST:
                    pe.wait_ge(tile_stored, (j + 1) * G)
                for k in range(2):
                    if b < LAST:
                        cols = adjT[:, 2 * b + k, :, :].rearrange("p i (v m r) -> p m v i r", v=V, m=M)[:, m, :, :, :]
                    else:
                        cols = adjT[:, 2 * b + k, m, :]
                    last = nc.tensor.matmul(h_ps[D * k:D * k + D, b, :], t_sb[:, m, :], cols,
                                            start=False, stop=(m == M - 1), skip_group_check=True)
                if m == M - 1:
                    last.then_inc(pair_spread, 1)

            def turn_over(j, more):
                def gather_more(c):
                    if more:
                        gather(j + 1, 0, c)

                turn_tile(j, 0)
                turn_tile(j, 1)
                turn_t(j, 0)
                turn_t(j, 1)
                gather_more(0)
                for half in range(2):
                    pe.wait_ge(t_ready, 2 * j + half + 1)
                    turn_tile(j, 2 + half)
                gather_more(1)
                turn_tile(j, 4)
                spread(j, 0, 0)
                turn_tile(j, 5)
                gather_more(2)
                spread(j, 0, 1)
                turn_tile(j, 6)
                gather_more(3)
                spread(j, 0, 2)
                turn_tile(j, 7)
                spread(j, 0, 3)

            for b in range(PAIRS):
                pe.wait_ge(e_ready, b + 1)
                for c in range(4):
                    gather(0, b, c)
            pe.wait_ge(constants_ready, 2)
            for b in range(PAIRS):
                nc.tensor.matmul(h_ps[:, b, :], zeros[:, 0:P], zeros[:, :], start=True, stop=True)

            with pe.Fori(1, BLOCKS) as j:
                turn_over(j - 1, True)
                for b in range(1, PAIRS):
                    for c in range(4):
                        gather(j, b, c)
                        spread(j - 1, b, c)

            def centre_h(b):
                if b == 0:
                    pe.wait_ge(centre_ready, 1)
                pe.wait_ge(hT_copied, b + 1)
                rows = h_ps[:, b, :].rearrange("p (s v f) -> p v s f", s=2, v=V)
                for v in range(V):
                    last = nc.tensor.matmul(rows[:, v, :, :], hT[:, b, P * v:P * v + P], centre[:, :, :],
                                            start=True, stop=True)
                last.then_inc(h_centred, 1)

            turn_over(BLOCKS - 1, False)
            for b in range(1, PAIRS):
                for m in range(M):
                    spread(BLOCKS - 1, b, m)
                centre_h(b - 1)
            centre_h(LAST)


_NAMES = ["x", "adj", "L0_gnn_W_u", "L0_gnn_diag_u", "L0_gnn_par_u", "L0_gnn_W_i", "L0_gnn_diag_i",
          "L0_gnn_par_i", "L0_gnn_ln_gamma", "L0_gnn_ln_beta"]


def kernel(**inputs):
    import numpy as np
    import concourse.bacc as bacc
    from concourse.bass_utils import run_bass_kernel_spmd

    nc = bacc.Bacc("TRN2", target_bir_lowering=False, num_devices=1)
    arrays, args = {}, []
    for name in _NAMES:
        a = np.ascontiguousarray(inputs[name])
        arrays[f"in_{name}"] = a
        args.append(nc.dram_tensor(f"in_{name}", a.shape, mybir.dt.from_np(a.dtype), kind="ExternalInput").ap())
    out = nc.dram_tensor("out_0", inputs["x"].shape, F32, kind="ExternalOutput").ap()
    build(nc, *args, out)
    r = run_bass_kernel_spmd(nc, [arrays], core_ids=[0])
    return r.results[0]["out_0"]
```

```python
from contextlib import ExitStack

import concourse.bass as bass
from concourse import mybir

F32 = mybir.dt.float32
BF16 = mybir.dt.bfloat16
ALU = mybir.AluOpType
ACT = mybir.ActivationFunctionType
AX_X = mybir.AxisListType.X

P = 128
S = 32
R = P // S
V = 4
QUAD = P * V
BLOCK = 512
M = BLOCK // P
EPS = 1e-5
PARTS = [(a, (a + d) % R) for d in range(R) for a in range(R)]
SHARES = ((8, 8, 0), (5, 7, 4), (5, 5, 6))
LOADED = 5
T_AFTER = 4


def build(nc, x, adj, W_u, diag_u, par_u, W_i, diag_i, par_i, gamma, beta, out):
    N, D = x.shape
    NU = diag_u.shape[0]
    QUADS = N // QUAD
    PAIRS = QUADS // 2
    LAST = PAIRS - 1
    VQ = QUADS - 1
    EXTRA = (5, 6)
    EXTRA_LAST = (5,)
    BLOCKS = N // BLOCK
    UQ = NU // QUAD
    UP = UQ // 2
    assert N % (2 * QUAD) == 0 and N % BLOCK == 0 and NU % (2 * QUAD) == 0 and 2 * D == P

    x_rows = x.rearrange("(q p v) f -> p q v f", p=P, v=V)
    out_rows = out.rearrange("(q p v) f -> p q v f", p=P, v=V)
    adj_rows = adj.rearrange("(q p v) c -> q p v c", p=P, v=V)

    with ExitStack() as ctx:
        def sb(name, shape, dt=F32):
            return ctx.enter_context(nc.sbuf_tensor(name, shape, dt))

        def sem(name):
            return ctx.enter_context(nc.semaphore(name))

        raw = sb("raw", [P, QUADS, V, BLOCK])
        adjT = sb("adjT", [P, QUADS, R, QUAD])
        squares = sb("squares", [P, 2, R, QUAD])
        x_sb = sb("x_sb", [P, QUADS, V, D])
        e_sb = sb("e_sb", [P, QUADS, V, D])
        tT_sb = sb("tT_sb", [P, BLOCK])
        t_sb = sb("t_sb", [P, M, D])
        ident = sb("ident", [P, P])
        centre = sb("centre", [P, 2, D])
        centre_g = sb("centre_g", [P, 2, D])
        centre_sum = sb("centre_sum", [P, 2])
        x2_sum = sb("x2_sum", [P, QUADS * V])
        root_set = sb("root_set", [P, 1])
        w2 = sb("w2", [P, 2, P])
        zeros = sb("zeros", [P, 512], BF16)
        scale = sb("scale", [P, QUADS, V])
        par = sb("par", [P, 2, 2])
        par01 = sb("par01", [P, 2])
        gb = sb("gb", [P, 2, D])
        eps = sb("eps", [P, 1])
        stat = sb("stat", [P, 6, QUADS, V])
        xT = adjT[:, 2 * LAST:QUADS, :, :].rearrange("p q i n -> p (q i) n")[:, 0:PAIRS, :]
        yT = e_sb[:, :, :, :].rearrange("p (b q) v f -> p b (q v f)", q=2)
        squares2 = raw[:, 2:4, :, :].rearrange("p q v (a n) -> p (q v a) n", a=2)[:, 0:QUADS, :]\
            .rearrange("p q (v f) -> p q v f", f=D)
        hT = raw[:, 0:2, :, :].rearrange("p q v c -> p (q v) c")[:, 0:PAIRS, :]

        h_ps = ctx.enter_context(nc.psum_tensor("h_ps", [P, PAIRS, 512], F32))
        t_ps = ctx.enter_context(nc.psum_tensor("t_ps", [P, BLOCK], F32))
        tr_ps = ctx.enter_context(nc.psum_tensor("tr_ps", [P, 2, 512], F32))

        raw_loaded = [sem(f"raw_loaded{q}") for q in range(QUADS)]
        x_loaded = sem("x_loaded")
        w_loaded = sem("w_loaded")
        scale_loaded = sem("scale_loaded")
        gb_loaded = sem("gb_loaded")
        w2_zeroed = sem("w2_zeroed")
        ident_zeroed = sem("ident_zeroed")
        ident_ready = sem("ident_ready")
        centre_set = sem("centre_set")
        centre_ready = sem("centre_ready")
        weighted = sem("weighted")
        centre_g_ready = sem("centre_g_ready")
        x2_centred = sem("x2_centred")
        constants_ready = sem("constants_ready")
        xT_done = sem("xT_done")
        xT_copied = sem("xT_copied")
        yT_done = sem("yT_done")
        yT_copied = sem("yT_copied")
        y_done = sem("y_done")
        y_scaled = sem("y_scaled")
        par_ready = sem("par_ready")
        scale_ready = sem("scale_ready")
        e_ready = sem("e_ready")
        x2_ready = sem("x2_ready")
        quad_gathered = sem("quad_gathered")
        pair_spread = sem("pair_spread")
        quad_squared = sem("quad_squared")
        vector_moved = sem("vector_moved")
        scalar_moved = sem("scalar_moved")
        rest_moved = [sem(f"rest_moved{q}") for q in range(VQ)]
        REST = 16 * SHARES[1][2]
        tile_turned = sem("tile_turned")
        tile_stored = sem("tile_stored")
        gather_done = sem("gather_done")
        gather_copied = sem("gather_copied")
        t_turned = sem("t_turned")
        t_ready = sem("t_ready")
        hT_copied = sem("hT_copied")
        h_centred = sem("h_centred")
        h_weighted = sem("h_weighted")
        squared1 = sem("squared1")
        summed1 = sem("summed1")
        rooted1 = sem("rooted1")
        inverted1 = sem("inverted1")
        scaled1 = sem("scaled1")
        added = [sem("pool_added"), sem("vector_added")]
        squared2 = sem("squared2")
        summed2 = sem("summed2")
        rooted2 = sem("rooted2")
        inverted2 = sem("inverted2")
        out_ready = [sem("pool_out_ready"), sem("vector_out_ready")]
        out_stored = sem("out_stored")

        block = ctx.enter_context(nc.Block())

        UNITS = [(2 * b, 2) for b in range(LAST)] + [(2 * LAST, 1), (2 * LAST + 1, 1)]
        PAIR_OF = [q // 2 for q, _ in UNITS]

        def rows(t, u):
            q, n = UNITS[u]
            return t[:, q:q + n, :, :].rearrange("p q v f -> p (q v) f")

        def in_bank(bank, u):
            q, n = UNITS[u]
            return bank[:, 256 * (q % 2):256 * (q % 2) + 256 * n].rearrange("p (g f) -> p g f", f=D)

        CENTRED = ((), (), (0,), (1, 2), (3, 4))
        COPIED = ((2,), (3,), (), (4,))
        POOLED = 3

        def finished(sems, u):
            return (sems[0], u + 1) if u < POOLED else (sems[1], u + 1 - POOLED)

        def row_stat(k, u):
            q, n = UNITS[u]
            return stat[:, k, q:q + n, :].rearrange("p q v -> p (q v)")

        def over_row(k, u):
            return row_stat(k, u).unsqueeze(2).to_broadcast([P, V * UNITS[u][1], D])

        def wait(eng, s, n):
            if not isinstance(n, int) or n > 0:
                eng.wait_ge(s, n)

        def couple(b, c):
            return 2 * b + c // 2, 2 * (c % 2)

        def first(j):
            return isinstance(j, int) and j == 0

        def last_block(j):
            return isinstance(j, int) and j == BLOCKS - 1

        def squared_quads(j):
            return [q for q in range(VQ) if not (first(j) and q in EXTRA or last_block(j) and q in EXTRA_LAST)]

        def turned_quads(j):
            return [q for q in range(QUADS) if q not in squared_quads(j)]

        def below(quads, q):
            return len([p for p in quads if p < q])

        def tiles_before(j, q):
            return (0 if first(j) else V * ((QUADS - VQ) * j + len(EXTRA))) + V * below(turned_quads(j), q)

        def squared_before(j, q):
            return (0 if first(j) else VQ * j - len(EXTRA)) + below(squared_quads(j), q)

        def place(j, odd, q):
            return ((0 if first(j) else VQ * odd - len(EXTRA)) + below(squared_quads(j), q)) % 2

        def rest_of(j, q):
            more = 16 * SHARES[2][2] - REST if last_block(j) else 0
            return REST * (j + 1 - (q in EXTRA)) + more

        def early_quads(j):
            return range(T_AFTER + 1)

        def later_quads(j):
            return [q for q in squared_quads(j) if q > T_AFTER]

        def early_shares(j, q):
            return first(j) and q < LOADED

        def shares(j, q):
            v, a, d = SHARES[0 if early_shares(j, q) else 2 if last_block(j) else 1]
            return PARTS[:v], PARTS[v:v + a], PARTS[v + a:]

        def bank(q, v):
            return (0, 0, 1, 0)[v] if q == VQ else v % 2

        def part(q, k, i, to):
            return squares[S * i:S * i + S, k, to, :], adjT[S * to:S * to + S, q, i, :]

        @block.sync
        def _(sp):
            def load(j, q):
                if not first(j) and q in squared_quads(j - 1):
                    if first(j - 1):
                        sp.wait_ge(quad_gathered, q + 1)
                elif not first(j):
                    sp.wait_ge(tile_turned, tiles_before(j - 1, q + 1))
                sp.dma_start(raw[:, q, :, :], adj_rows[q, :, :, bass.ds(j * BLOCK, BLOCK)])\
                    .then_inc(raw_loaded[q], 16)

            def move(j, odd, q):
                for i, to in shares(j, q)[2]:
                    src, dst = part(q, place(j, odd, q), i, to)
                    sp.dma_start(dst, src).then_inc(rest_moved[q], 16)

            sp.dma_start(x_sb[:, :, :, :], x_rows).then_inc(x_loaded, 16)
            sp.wait_ge(w2_zeroed, 1)
            for k, w in enumerate((W_u, W_i)):
                for a in range(2):
                    sp.dma_start(w2[D * a:D * a + D, k, D * a:D * a + D], w).then_inc(w_loaded, 16)
            for q in range(QUADS):
                load(0, q)

            def whole_block(j, odd):
                for q in LOAD_ORDER:
                    if q in squared_quads(j):
                        sp.wait_ge(quad_squared, squared_before(j, q) + 1)
                        move(j, odd, q)
                    load(j + 1, q)

            LOAD_ORDER = [*range(VQ - 2), VQ, VQ - 2, VQ - 1]
            whole_block(0, 0)
            with sp.Fori(1, BLOCKS - 2, 2) as j:
                whole_block(j, 1)
                whole_block(j + 1, 0)
            for q in squared_quads(BLOCKS - 1):
                sp.wait_ge(quad_squared, squared_before(BLOCKS - 1, q) + 1)
                move(BLOCKS - 1, (BLOCKS - 1) % 2, q)
            for u, (q, n) in enumerate(UNITS):
                sp.wait_ge(*finished(out_ready, u))
                sp.dma_start(out_rows[:, q:q + n, :, :], e_sb[:, q:q + n, :, :]).then_inc(out_stored, 16)
            sp.wait_ge(out_stored, 16 * len(UNITS))

        @block.gpsimd
        def _(pool):
            nc.gpsimd.memset(ident[:, :], 0.0).then_inc(ident_zeroed, 1)
            nc.gpsimd.memset(w2[:, :, :], 0.0).then_inc(w2_zeroed, 1)
            pool.wait_ge(ident_zeroed, 1)
            nc.gpsimd.affine_select(out=ident[:, :], in_=ident[:, :], compare_op=ALU.not_equal, fill=1.0,
                                    base=0, pattern=[[-1, P]], channel_multiplier=1).then_inc(ident_ready, 1)
            for k, g in enumerate((gamma, beta)):
                pool.dma_start(gb[:, k, :], g.partition_broadcast(P)).then_inc(gb_loaded, 16)
            for b in range(PAIRS):
                pool.wait_ge(y_scaled, b + 1)
                s = e_sb[:, 2 * b:2 * b + 2, :, :]
                nc.gpsimd.tensor_tensor(s, s, x_sb[:, 2 * b:2 * b + 2, :, :], ALU.add).then_inc(e_ready, 1)
            pool.wait_ge(e_ready, PAIRS)
            x2 = x_sb[:, :, :, :].rearrange("p q v f -> p (q v) f")
            nc.gpsimd.tensor_tensor(x2, x2, x2, ALU.add).then_inc(x2_ready, 1)
            pool.wait_ge(gb_loaded, 16 * 2)
            pool.wait_ge(x2_ready, 1)
            nc.gpsimd.tensor_tensor(x2, x2, gb[:, 1:2, :].to_broadcast([P, QUADS * V, D]), ALU.add)\
                .then_inc(x2_ready, 1)
            nc.gpsimd.memset(centre[:, :, :], 0.0).then_inc(centre_set, 1)
            pool.wait_ge(centre_set, 1)
            for a in range(2):
                nc.gpsimd.memset(centre[D * a:D * a + D, a, :], -1.0 / D).then_inc(centre_set, 1)
            pool.wait_ge(centre_set, 3)
            cc = centre[:, :, :].rearrange("p a f -> p (a f)")
            nc.gpsimd.tensor_tensor(cc, cc, ident[:, :], ALU.add).then_inc(centre_ready, 1)

            def add_x(u):
                pool.wait_ge(scaled1, u + 1)
                nc.gpsimd.tensor_tensor(rows(e_sb, u), rows(e_sb, u), rows(x_sb, u), ALU.add)\
                    .then_inc(added[0], 1)

            def scale2(u):
                pool.wait_ge(inverted2, u + 1)
                nc.gpsimd.tensor_tensor(rows(e_sb, u), rows(e_sb, u), over_row(5, u), ALU.mult)\
                    .then_inc(out_ready[0], 1)

            pool.wait_ge(x2_centred, 1)
            for b in range(POOLED + 1):
                if b < POOLED:
                    add_x(b)
                if b > 0:
                    scale2(b - 1)


        @block.scalar
        def _(act):
            for k, p in enumerate((par_u, par_i)):
                act.dma_start(par[:, k, :], p.partition_broadcast(P)).then_inc(scale_loaded, 16)
            for a, b, d in ((0, UQ, diag_u), (UQ, QUADS, diag_i)):
                act.dma_start(scale[:, a:b, :], d.rearrange("(q p v) -> p q v", p=P, v=V)).then_inc(scale_loaded, 16)
            act.wait_ge(constants_ready, 2)
            nc.scalar.activation(root_set[:, :], eps[:, :], ACT.Sqrt)
            for b in range(PAIRS):
                act.wait_ge(xT_done, b + 1)
                nc.scalar.copy(xT[:, b, :], h_ps[:, b, :]).then_inc(xT_copied, 1)
            for b in range(PAIRS):
                act.wait_ge(yT_done, b + 1)
                nc.scalar.copy(yT[:, b, :], h_ps[:, b, :]).then_inc(yT_copied, 1)

            def move(j, odd, q, a=0, b=R * R):
                mine = shares(j, q)[1]
                for n in range(a, min(b, len(mine))):
                    if n == 0:
                        act.wait_ge(quad_squared, squared_before(j, q) + 1)
                    src, dst = part(q, place(j, odd, q), *mine[n])
                    copied = nc.scalar.copy(dst, src)
                    if n == len(mine) - 2 and early_shares(j, q):
                        copied.then_inc(rest_moved[q], REST)
                    if n == len(mine) - 1:
                        copied.then_inc(scalar_moved, 1)

            def store(j, q, v):
                act.wait_ge(tile_turned, tiles_before(j, q) + v + 1)
                nc.scalar.copy(adjT[:, q, :, v * P:v * P + P].rearrange("p i (m r) -> p m i r", m=M),
                               tr_ps[:, bank(q, v), :].rearrange("p (m i r) -> p m i r", m=M, i=R)).then_inc(tile_stored, 1)

            def copy_hT(b):
                act.wait_ge(pair_spread, PAIRS * (BLOCKS - 1) + b + 1)
                nc.scalar.copy(hT[:, b, :], h_ps[:, b, :]).then_inc(hT_copied, 1)

            def whole_block(j, odd):
                for q in early_quads(j)[:-1]:
                    move(j, odd, q)
                q = early_quads(j)[-1]
                for turned in turned_quads(j)[:-1]:
                    for v in range(V):
                        store(j, turned, v)
                store(j, VQ, 0)
                move(j, odd, q, 0, 2)
                store(j, VQ, 1)
                store(j, VQ, 2)
                move(j, odd, q, 2)
                store(j, VQ, 3)
                for q in later_quads(j):
                    if last_block(j) and q == VQ - 1:
                        copy_hT(0)
                    move(j, odd, q)

            whole_block(0, 0)
            with act.Fori(1, BLOCKS - 2, 2) as j:
                whole_block(j, 1)
                whole_block(j + 1, 0)
            whole_block(BLOCKS - 1, (BLOCKS - 1) % 2)

            def square1(u):
                act.wait_ge(h_centred, PAIR_OF[u] + 1)
                nc.scalar.activation(rows(e_sb, u), in_bank(h_ps[:, PAIR_OF[u], :], u), ACT.Square)\
                    .then_inc(squared1, 1)

            def square2(u):
                act.wait_ge(*finished(added, u))
                nc.scalar.activation(rows(squares2, u), rows(e_sb, u), ACT.Square).then_inc(squared2, 1)

            def root(u, of, to):
                return nc.scalar.activation(row_stat(to, u), row_stat(of, u), ACT.Sqrt,
                                            bias=eps[:, :], scale=1.0 / D)

            def root1(u):
                act.wait_ge(summed1, u + 1)
                root(u, 0, 1).then_inc(rooted1, 1)

            def root2(u):
                act.wait_ge(summed2, u + 1)
                root(u, 3, 4).then_inc(rooted2, 1)

            copy_hT(1)
            for b in range(LAST):
                for copied in COPIED[b]:
                    copy_hT(copied)
                square1(b)
                if b > 0:
                    square2(b - 1)
                root1(b)
                if b > 0:
                    root2(b - 1)
            square1(LAST)
            square1(LAST + 1)
            square2(LAST - 1)
            root1(LAST)
            root1(LAST + 1)
            root2(LAST - 1)
            square2(LAST)
            square2(LAST + 1)
            root2(LAST)
            root2(LAST + 1)

        @block.vector
        def _(dve):
            nc.vector.memset(zeros[:, :], 0.0).then_inc(constants_ready, 1)
            nc.vector.memset(eps[:, :], EPS).then_inc(constants_ready, 1)

            def turn_squares(k, q, v, to):
                return nc.vector.transpose(
                    squares[:, k, :, P * v:P * to].rearrange("p t (a r) -> p a t r", r=S),
                    raw[:, q, v:to, :].rearrange("p v (m t c) -> p (v m) t c", t=R, c=S))

            def square(j, odd, q, halves=(0, 1)):
                k = place(j, odd, q)
                if halves == (1,):
                    turn_squares(k, q, 2, V).then_inc(quad_squared, 1)
                    return
                dve.wait_ge(raw_loaded[q], 16 * (j + 1))
                if not first(j) and (q % 2 == 0 or q - 1 not in squared_quads(j)):
                    dve.wait_ge(pair_spread, (j - 1) * PAIRS + q // 2 + 1)
                n = squared_before(j, q) - 1
                wait(dve, vector_moved, n)
                wait(dve, scalar_moved, n)
                if q >= 2:
                    before = squared_quads(j)[below(squared_quads(j), q) - 2]
                    dve.wait_ge(rest_moved[before], rest_of(j, before))
                elif not first(j):
                    before = VQ + q - 2
                    dve.wait_ge(rest_moved[before], rest_of(j - 1, before))
                if halves == (0, 1):
                    turn_squares(k, q, 0, V).then_inc(quad_squared, 1)
                else:
                    turn_squares(k, q, 0, 2)

            def move(j, odd, q):
                dve.wait_ge(quad_squared, squared_before(j, q) + 1)
                for i, to in shares(j, q)[0]:
                    src, dst = part(q, place(j, odd, q), i, to)
                    moved = nc.vector.tensor_copy(dst, src)
                moved.then_inc(vector_moved, 1)

            def copy_t(j):
                dve.wait_ge(gather_done, j + 1)
                nc.vector.tensor_copy(tT_sb[:, :], t_ps[:, :]).then_inc(gather_copied, 1)

            def finish_t(j):
                dve.wait_ge(t_turned, j + 1)
                nc.vector.tensor_reduce(t_sb[:, :, :], tr_ps[:, 1, :].rearrange("p (m s f) -> p m f s", m=M, s=2),
                                        AX_X, ALU.add).then_inc(t_ready, 1)

            LANDED = range(1)
            for q in LANDED:
                square(0, 0, q)
                move(0, 0, q)
            dve.wait_ge(scale_loaded, 16 * 4)
            nc.vector.tensor_tensor(par01[:, :], par[:, :, 0], par[:, :, 1], ALU.mult).then_inc(par_ready, 1)
            dve.wait_ge(par_ready, 1)
            for k, (a, b) in enumerate(((0, UQ), (UQ, QUADS))):
                nc.vector.tensor_scalar(scale[:, a:b, :], scale[:, a:b, :], par01[:, k:k + 1], None,
                                        ALU.mult).then_inc(scale_ready, 1)
            dve.wait_ge(scale_ready, 2)
            for b in range(PAIRS):
                dve.wait_ge(y_done, b + 1)
                s = scale[:, 2 * b:2 * b + 2, :].rearrange("p q v -> p (q v)").unsqueeze(2).to_broadcast([P, 2 * V, D])
                nc.vector.tensor_tensor(e_sb[:, 2 * b:2 * b + 2, :, :].rearrange("p q v f -> p (q v) f"),
                                        h_ps[:, b, :].rearrange("p (g f) -> p g f", f=D), s,
                                        ALU.mult).then_inc(y_scaled, 1)

            def prepare_end():
                dve.wait_ge(gb_loaded, 16 * 2)
                dve.wait_ge(centre_ready, 1)
                nc.vector.tensor_tensor(centre_g[:, :, :], centre[:, :, :], gb[:, 0:1, :].to_broadcast([P, 2, D]),
                                        ALU.mult).then_inc(weighted, 1)
                x2 = x_sb[:, :, :, :].rearrange("p q v f -> p (q v) f")
                dve.wait_ge(x2_ready, 2)
                nc.vector.tensor_reduce(x2_sum[:, :], x2, AX_X, ALU.add).then_inc(weighted, 1)
                dve.wait_ge(weighted, 2)
                nc.vector.tensor_reduce(centre_sum[:, :], centre_g[:, :, :], AX_X, ALU.add).then_inc(weighted, 1)
                dve.wait_ge(weighted, 3)
                nc.vector.scalar_tensor_tensor(centre_g[:, :, :], centre_sum[:, :].unsqueeze(2).to_broadcast([P, 2, D]),
                                               -1.0 / D, centre_g[:, :, :], ALU.mult, ALU.add)\
                    .then_inc(centre_g_ready, 1)
                nc.vector.scalar_tensor_tensor(x2, x2_sum[:, :].unsqueeze(2).to_broadcast([P, QUADS * V, D]),
                                               -1.0 / D, x2, ALU.mult, ALU.add).then_inc(x2_centred, 1)

            def whole_block(j, odd):
                for q in early_quads(j)[:-1]:
                    if not (first(j) and q in LANDED):
                        square(j, odd, q)
                        move(j, odd, q)
                q = early_quads(j)[-1]
                if first(j):
                    square(j, odd, q)
                    move(j, odd, q)
                    copy_t(j)
                    prepare_end()
                    finish_t(j)
                else:
                    square(j, odd, q, (0,))
                    copy_t(j)
                    square(j, odd, q, (1,))
                    finish_t(j)
                    move(j, odd, q)
                for q in later_quads(j):
                    square(j, odd, q)
                    move(j, odd, q)

            whole_block(0, 0)
            with dve.Fori(1, BLOCKS - 2, 2) as j:
                whole_block(j, 1)
                whole_block(j + 1, 0)
            whole_block(BLOCKS - 1, (BLOCKS - 1) % 2)

            def first_norm(u):
                dve.wait_ge(squared1, u + 1)
                nc.vector.tensor_reduce(row_stat(0, u), rows(e_sb, u), AX_X, ALU.add).then_inc(summed1, 1)

            def add_x(u):
                dve.wait_ge(rooted1, u + 1)
                nc.vector.reciprocal(row_stat(2, u), row_stat(1, u)).then_inc(inverted1, 1)
                dve.wait_ge(inverted1, u + 1)
                dve.wait_ge(h_weighted, PAIR_OF[u] + 1)
                nc.vector.tensor_tensor(rows(e_sb, u), in_bank(tr_ps[:, PAIR_OF[u] % 2, :], u), over_row(2, u),
                                        ALU.mult).then_inc(scaled1, 1)
                if u >= POOLED:
                    dve.wait_ge(scaled1, u + 1)
                    nc.vector.tensor_tensor(rows(e_sb, u), rows(e_sb, u), rows(x_sb, u), ALU.add)\
                        .then_inc(added[1], 1)

            def second_norm(u):
                dve.wait_ge(squared2, u + 1)
                nc.vector.tensor_reduce(row_stat(3, u), rows(squares2, u), AX_X, ALU.add).then_inc(summed2, 1)

            def finish(u):
                dve.wait_ge(rooted2, u + 1)
                nc.vector.reciprocal(row_stat(5, u), row_stat(4, u)).then_inc(inverted2, 1)
                if u >= POOLED:
                    dve.wait_ge(inverted2, u + 1)
                    nc.vector.tensor_tensor(rows(e_sb, u), rows(e_sb, u), over_row(5, u), ALU.mult)\
                        .then_inc(out_ready[1], 1)

            dve.wait_ge(x2_centred, 1)
            for b in range(LAST):
                first_norm(b)
                if b > 0:
                    second_norm(b - 1)
                add_x(b)
                if b > 0:
                    finish(b - 1)
            first_norm(LAST)
            first_norm(LAST + 1)
            add_x(LAST)
            second_norm(LAST - 1)
            add_x(LAST + 1)
            finish(LAST - 1)
            second_norm(LAST)
            second_norm(LAST + 1)
            finish(LAST)
            finish(LAST + 1)

        @block.tensor
        def _(pe):
            pe.wait_ge(ident_ready, 1)
            pe.wait_ge(x_loaded, 16)
            for b in range(PAIRS):
                for c in range(4):
                    q, v = couple(b, c)
                    last = nc.tensor.transpose(h_ps[:, b, P * c:P * c + P],
                                               x_sb[:, q, v:v + 2, :].rearrange("p v f -> p (v f)"), ident[:, :])
                last.then_inc(xT_done, 1)
            pe.wait_ge(w_loaded, 16 * 4)
            for b in range(PAIRS):
                pe.wait_ge(xT_copied, b + 1)
                nc.tensor.matmul(h_ps[:, b, :], w2[:, 0 if b < UP else 1, :], xT[:, b, :],
                                 start=True, stop=True).then_inc(yT_done, 1)
            for b in range(PAIRS):
                pe.wait_ge(yT_copied, b + 1)
                for c in range(4):
                    last = nc.tensor.transpose(h_ps[:, b, P * c:P * c + P], yT[:, b, P * c:P * c + P], ident[:, :])
                last.then_inc(y_done, 1)

            def gather(j, b, c):
                q, v = couple(b, c)
                if c % 2 == 0:
                    pe.wait_ge(raw_loaded[q], 16 * (j + 1))
                for k in range(2):
                    last = nc.tensor.matmul(t_ps[D * k:D * k + D, :], e_sb[:, q, v + k, :], raw[:, q, v + k, :],
                                            start=(b == 0 and c == 0), stop=(b == LAST and c == 3))
                if b == LAST and c == 3:
                    last.then_inc(gather_done, 1)
                elif c % 2 == 1 and first(j):
                    last.then_inc(quad_gathered, 1)

            def turn_tile(j, q, v):
                if q == VQ and v == 2:
                    pe.wait_ge(t_ready, j + 1)
                elif q == VQ and v > 0:
                    pe.wait_ge(tile_stored, tiles_before(j, q) + (v + 1) // 2)
                elif v >= 2 or q > turned_quads(j)[0]:
                    pe.wait_ge(tile_stored, tiles_before(j, q) + v - 1)
                for m in range(M):
                    last = nc.tensor.transpose(tr_ps[:, bank(q, v), P * m:P * m + P],
                                               raw[:, q, v, P * m:P * m + P], ident[:, :])
                last.then_inc(tile_turned, 1)

            def turn_t(j):
                pe.wait_ge(gather_copied, j + 1)
                if turned_quads(j)[0] < VQ:
                    pe.wait_ge(tile_stored, tiles_before(j, VQ))
                for m in range(M):
                    last = nc.tensor.transpose(tr_ps[:, 1, P * m:P * m + P], tT_sb[:, P * m:P * m + P], ident[:, :])
                last.then_inc(t_turned, 1)

            def spread(j, b, m):
                for q in (2 * b, 2 * b + 1) if m == 0 else ():
                    if q in squared_quads(j):
                        pe.wait_ge(vector_moved, squared_before(j, q + 1))
                        pe.wait_ge(scalar_moved, squared_before(j, q + 1))
                        pe.wait_ge(rest_moved[q], rest_of(j, q))
                    else:
                        pe.wait_ge(tile_stored, tiles_before(j, q + 1))
                for k in range(2):
                    cols = adjT[:, 2 * b + k, :, :].rearrange("p i (v m r) -> p m v i r", v=V, m=M)[:, m, :, :, :]
                    last = nc.tensor.matmul(h_ps[D * k:D * k + D, b, :], t_sb[:, m, :], cols,
                                            start=False, stop=(m == M - 1), skip_group_check=True)
                if m == M - 1:
                    last.then_inc(pair_spread, 1)

            def turn_over(j):
                def gather_next(c):
                    if not last_block(j):
                        gather(j + 1, 0, c)

                for q in turned_quads(j)[:-1]:
                    for v in range(V):
                        turn_tile(j, q, v)
                turn_tile(j, VQ, 0)
                turn_t(j)
                gather_next(0)
                turn_tile(j, VQ, 1)
                turn_tile(j, VQ, 2)
                gather_next(1)
                turn_tile(j, VQ, 3)
                spread(j, 0, 0)
                gather_next(2)
                spread(j, 0, 1)
                gather_next(3)
                spread(j, 0, 2)
                spread(j, 0, 3)

            for b in range(PAIRS):
                pe.wait_ge(e_ready, b + 1)
                for c in range(4):
                    gather(0, b, c)
            pe.wait_ge(constants_ready, 2)
            for b in range(PAIRS):
                nc.tensor.matmul(h_ps[:, b, :], zeros[:, 0:P], zeros[:, :], start=True, stop=True)

            def whole_block(j):
                turn_over(j - 1)
                for b in range(1, PAIRS):
                    for c in range(4):
                        gather(j, b, c)
                        spread(j - 1, b, c)

            whole_block(1)
            with pe.Fori(2, BLOCKS) as j:
                whole_block(j)

            def centre_h(b):
                if b == 0:
                    pe.wait_ge(centre_g_ready, 1)
                    pe.wait_ge(tile_stored, tiles_before(BLOCKS - 1, QUADS))
                pe.wait_ge(hT_copied, b + 1)
                for to, matrix, done in ((h_ps[:, b, :], centre, h_centred), (tr_ps[:, b % 2, :], centre_g, h_weighted)):
                    if matrix is centre_g and b >= 2:
                        pe.wait_ge(scaled1, b - 1)
                    for v in range(V):
                        last = nc.tensor.matmul(to.rearrange("p (s v f) -> p v s f", s=2, v=V)[:, v, :, :],
                                                hT[:, b, P * v:P * v + P], matrix[:, :, :], start=True, stop=True)
                    last.then_inc(done, 1)

            turn_over(BLOCKS - 1)
            for b in range(1, PAIRS):
                for m in range(M):
                    spread(BLOCKS - 1, b, m)
                for centred in CENTRED[b]:
                    centre_h(centred)


_NAMES = ["x", "adj", "L0_gnn_W_u", "L0_gnn_diag_u", "L0_gnn_par_u", "L0_gnn_W_i", "L0_gnn_diag_i",
          "L0_gnn_par_i", "L0_gnn_ln_gamma", "L0_gnn_ln_beta"]


def kernel(**inputs):
    import numpy as np
    import concourse.bacc as bacc
    from concourse.bass_utils import run_bass_kernel_spmd

    nc = bacc.Bacc("TRN2", target_bir_lowering=False, num_devices=1)
    arrays, args = {}, []
    for name in _NAMES:
        a = np.ascontiguousarray(inputs[name])
        arrays[f"in_{name}"] = a
        args.append(nc.dram_tensor(f"in_{name}", a.shape, mybir.dt.from_np(a.dtype), kind="ExternalInput").ap())
    out = nc.dram_tensor("out_0", inputs["x"].shape, F32, kind="ExternalOutput").ap()
    build(nc, *args, out)
    r = run_bass_kernel_spmd(nc, [arrays], core_ids=[0])
    return r.results[0]["out_0"]
```
